# Optimizing a Trainium2 kernel written in Bass

```python
import numpy as np
import jax
import jax.numpy as jnp

def _softmax(x, axis=-1):
    return jax.nn.softmax(x, axis=axis)

def _gelu(x):
    return jax.nn.gelu(x, approximate=True)

def _silu(x):
    return jax.nn.silu(x)

def _sigmoid(x):
    return jax.nn.sigmoid(x)

def _layernorm(x, axis=-1, eps=1e-05):
    m = jnp.mean(x, axis=axis, keepdims=True)
    v = jnp.var(x, axis=axis, keepdims=True)
    return (x - m) / jnp.sqrt(v + eps)

def _scatter_add(tgt, idx, src, axis=0):
    return tgt.at[idx].add(src)

def _segment_sum(src, seg, n):
    return jax.ops.segment_sum(src, seg, n)
kernel_name = 'mk_perceiver_d1_seqx_r2_ab978f'

def setup_inputs(seed: int=0):
    np.random.seed(seed)
    _w = jnp.asarray

    def _rec_inputs():
        import jax
        import jax.numpy as jnp
        _rk = jax.random.key(seed)
        x = 7.22e-05 + 1 * jax.random.normal(jax.random.fold_in(_rk, 1), (4, 128, 512), jnp.float32)
        _lenS = 128 - jax.random.randint(jax.random.fold_in(_rk, 7), (4,), 0, max(1, 128 // 4) + 1, jnp.int32)
        _lenS2 = 2048 - jax.random.randint(jax.random.fold_in(_rk, 8), (4,), 0, max(1, 2048 // 4) + 1, jnp.int32)
        _ctx_768P = jax.random.normal(jax.random.fold_in(_rk, 11), (4, 16, 384), jnp.float32)
        _ctx_768c = jax.random.dirichlet(jax.random.fold_in(_rk, 511), 0.3 * jnp.ones((16,), jnp.float32), (4, 2048))
        _ctx_768t = jnp.einsum('bsk,bkd->bsd', _ctx_768c, _ctx_768P)
        _ctx_768t = _ctx_768t * jax.lax.rsqrt(jnp.mean(jnp.square(_ctx_768t)) + 1e-12) * 0.953939
        ctx_768 = 3.88148e-05 + 0.999967 * (_ctx_768t + 0.3 * jax.random.normal(jax.random.fold_in(_rk, 611), (4, 2048, 384), jnp.float32))
        _validS = jnp.arange(128)[None, :] < _lenS[:, None]
        _validS2 = jnp.arange(2048)[None, :] < _lenS2[:, None]
        _causal = jnp.tril(jnp.ones((128, 128), dtype=bool))
        mask_BxS_bf1 = jnp.ones((4, 128), dtype=bool)
        mask_BxS2_bf1 = jnp.ones((4, 2048), dtype=bool)
        return (x, ctx_768, mask_BxS_bf1, mask_BxS2_bf1)
    x, ctx_768, mask_BxS_bf1, mask_BxS2_bf1 = _rec_inputs()

    def _L0_xattn_setup():
        import jax, jax.numpy as jnp
        import numpy as np
        B, T, DT, G, DV = (16, 256, 512, 288, 384)
        H, DH = (4, 32)
        INNER = H * DH
        HID = 4 * DT
        N_STATE = 64
        K_TOP = 32

        def layernorm(x, g, b, eps=1e-05):
            m = x.mean(-1, keepdims=True)
            v = x.var(-1, keepdims=True)
            return (x - m) * jax.lax.rsqrt(v + eps) * g + b

        def s4d(x, log_dt, A_re, A_im, C_re, C_im, D_skip):
            Bb, L, D = x.shape
            dt = jnp.exp(log_dt)
            A = A_re + 1j * A_im
            C = C_re + 1j * C_im
            dtA = dt[:, None] * A
            dC = C * (jnp.exp(dtA) - 1.0) / A
            powers = jnp.exp(dtA[:, :, None] * jnp.arange(L))
            K = 2.0 * jnp.einsum('dn,dnl->dl', dC, powers).real
            n = 2 * L
            Kf = jnp.fft.rfft(K, n=n, axis=-1)
            xf = jnp.fft.rfft(x, n=n, axis=1)
            y = jnp.fft.irfft(xf * Kf.T[None], n=n, axis=1)[:, :L]
            return y + x * D_skip
        key = jax.random.key(seed)
        ks = jax.random.split(key, 16)
        s = 0.02
        inp = {'x_text': jax.random.normal(ks[0], (B, T, DT), jnp.float32), 'x_vision': jax.random.normal(ks[1], (B, G, DV), jnp.float32), 'text_mask': jnp.ones((B, T), bool), 'vision_mask': jnp.ones((B, G), bool), 'Wq': jax.random.normal(ks[2], (DT, INNER), jnp.float32) * s, 'Wk': jax.random.normal(ks[3], (DV, INNER), jnp.float32) * s, 'Wv': jax.random.normal(ks[4], (DV, DT), jnp.float32) * s, 'W_film_in': jax.random.normal(ks[5], (DT, 2 * DT), jnp.float32) * s, 'b_film_in': jnp.zeros((2 * DT,), jnp.float32), 'W_film_out': jax.random.normal(ks[6], (DT, 2 * DT), jnp.float32) * s, 'b_film_out': jnp.zeros((2 * DT,), jnp.float32), 'g_norm_in': jnp.ones((DT,), jnp.float32), 'b_norm_in': jnp.zeros((DT,), jnp.float32), 'g_norm_out': jnp.ones((DT,), jnp.float32), 'b_norm_out': jnp.zeros((DT,), jnp.float32), 'g_ffn': jnp.ones((DT,), jnp.float32), 'b_ffn': jnp.zeros((DT,), jnp.float32), 'W1': jax.random.normal(ks[7], (DT, HID), jnp.float32) * s, 'b1': jnp.zeros((HID,), jnp.float32), 'W2': jax.random.normal(ks[8], (HID, DT), jnp.float32) * s, 'b2': jnp.zeros((DT,), jnp.float32), 'log_dt': jnp.log(0.001) + jax.random.uniform(ks[9], (DT,), jnp.float32) * (jnp.log(0.1) - jnp.log(0.001)), 'A_re': -0.5 * jnp.ones((DT, N_STATE), jnp.float32), 'A_im': jnp.tile(jnp.pi * jnp.arange(N_STATE, dtype=jnp.float32), (DT, 1)), 'C_re': jax.random.normal(ks[10], (DT, N_STATE), jnp.float32) * 0.5 ** 0.5, 'C_im': jax.random.normal(ks[11], (DT, N_STATE), jnp.float32) * 0.5 ** 0.5, 'D_skip': jax.random.normal(ks[12], (DT,), jnp.float32), 'mod_gate': jnp.array(0.5, jnp.float32)}
        return inp
    _L0_xattn_all = _L0_xattn_setup()
    _L0_xattn_in = {k: v for k, v in _L0_xattn_all.items() if k in ('Wq', 'Wk', 'Wv', 'W_film_in', 'b_film_in', 'W_film_out', 'b_film_out', 'g_norm_in', 'b_norm_in', 'g_norm_out', 'b_norm_out', 'g_ffn', 'b_ffn', 'W1', 'b1', 'W2', 'b2', 'log_dt', 'A_re', 'A_im', 'C_re', 'C_im', 'D_skip', 'mod_gate')}
    del _L0_xattn_all

    def _L0_attn_setup():
        import jax, jax.numpy as jnp
        import numpy as np
        EMBED_DIM = 512
        NUM_HEADS = 16
        HEAD_DIM = EMBED_DIM // NUM_HEADS
        WINDOW_SIZE = 128
        SCALE = 1.0 / np.sqrt(HEAD_DIM)

        def _band_mask(T):
            i = jnp.arange(T)[:, None]
            j = jnp.arange(T)[None, :]
            full = j > i
            band = full & (j >= i - (WINDOW_SIZE - 1))
            return band
        key = jax.random.key(seed)
        kx, kq, kk, kv, ko = jax.random.split(key, 5)
        B, T, C = (2, 1024, EMBED_DIM)
        x = jax.random.normal(kx, (B, T, C), dtype=jnp.float32)
        s = 1.0 / np.sqrt(C)
        Wq = jax.random.uniform(kq, (C, C), dtype=jnp.float32, minval=-s, maxval=s)
        Wk = jax.random.uniform(kk, (C, C), dtype=jnp.float32, minval=-s, maxval=s)
        Wv = jax.random.uniform(kv, (C, C), dtype=jnp.float32, minval=-s, maxval=s)
        Wo = jax.random.uniform(ko, (C, C), dtype=jnp.float32, minval=-s, maxval=s)
        return {'x': x, 'Wq': Wq, 'Wk': Wk, 'Wv': Wv, 'Wo': Wo}
    _L0_attn_all = _L0_attn_setup()
    _L0_attn_in = {k: v for k, v in _L0_attn_all.items() if k in ('Wq', 'Wk', 'Wv', 'Wo')}
    del _L0_attn_all

    def _L0_ffn_setup():
        import jax, jax.numpy as jnp
        import numpy as np
        D_MODEL = 512
        D_FF = 1024
        NUM_EXPERTS = 16
        TOP_K = 2
        CAPACITY_FACTOR = 1.25
        BATCH, SEQ = (4, 1024)
        key = jax.random.key(seed)
        k0, k1, k2, k3 = jax.random.split(key, 4)
        x = jax.random.normal(k0, (BATCH, SEQ, D_MODEL), jnp.float32)
        gate_w = jax.random.normal(k1, (NUM_EXPERTS, D_MODEL), jnp.float32) / np.float32(np.sqrt(D_MODEL))
        w1 = jax.random.normal(k2, (NUM_EXPERTS, D_MODEL, D_FF), jnp.float32) / np.float32(np.sqrt(D_MODEL))
        w2 = jax.random.normal(k3, (NUM_EXPERTS, D_FF, D_MODEL), jnp.float32) / np.float32(np.sqrt(D_FF))
        return {'x': x, 'gate_w': gate_w, 'w1': w1, 'w2': w2}
    _L0_ffn_all = _L0_ffn_setup()
    _L0_ffn_in = {k: v for k, v in _L0_ffn_all.items() if k in ('gate_w', 'w1', 'w2')}
    del _L0_ffn_all
    return {'x': x, 'ctx_768': ctx_768, 'mask_BxS_bf1': mask_BxS_bf1, 'mask_BxS2_bf1': mask_BxS2_bf1, 'L0_xattn_Wq': _L0_xattn_in['Wq'], 'L0_xattn_Wk': _L0_xattn_in['Wk'], 'L0_xattn_Wv': _L0_xattn_in['Wv'], 'L0_xattn_W_film_in': _L0_xattn_in['W_film_in'], 'L0_xattn_b_film_in': _L0_xattn_in['b_film_in'], 'L0_xattn_W_film_out': _L0_xattn_in['W_film_out'], 'L0_xattn_b_film_out': _L0_xattn_in['b_film_out'], 'L0_xattn_g_norm_in': _L0_xattn_in['g_norm_in'], 'L0_xattn_b_norm_in': _L0_xattn_in['b_norm_in'], 'L0_xattn_g_norm_out': _L0_xattn_in['g_norm_out'], 'L0_xattn_b_norm_out': _L0_xattn_in['b_norm_out'], 'L0_xattn_g_ffn': _L0_xattn_in['g_ffn'], 'L0_xattn_b_ffn': _L0_xattn_in['b_ffn'], 'L0_xattn_W1': _L0_xattn_in['W1'], 'L0_xattn_b1': _L0_xattn_in['b1'], 'L0_xattn_W2': _L0_xattn_in['W2'], 'L0_xattn_b2': _L0_xattn_in['b2'], 'L0_xattn_log_dt': _L0_xattn_in['log_dt'], 'L0_xattn_A_re': _L0_xattn_in['A_re'], 'L0_xattn_A_im': _L0_xattn_in['A_im'], 'L0_xattn_C_re': _L0_xattn_in['C_re'], 'L0_xattn_C_im': _L0_xattn_in['C_im'], 'L0_xattn_D_skip': _L0_xattn_in['D_skip'], 'L0_xattn_mod_gate': _L0_xattn_in['mod_gate'], 'L0_attn_Wq': _L0_attn_in['Wq'], 'L0_attn_Wk': _L0_attn_in['Wk'], 'L0_attn_Wv': _L0_attn_in['Wv'], 'L0_attn_Wo': _L0_attn_in['Wo'], 'L0_ffn_gate_w': _L0_ffn_in['gate_w'], 'L0_ffn_w1': _L0_ffn_in['w1'], 'L0_ffn_w2': _L0_ffn_in['w2']}

def reference(x, ctx_768, mask_BxS_bf1, mask_BxS2_bf1, L0_xattn_Wq, L0_xattn_Wk, L0_xattn_Wv, L0_xattn_W_film_in, L0_xattn_b_film_in, L0_xattn_W_film_out, L0_xattn_b_film_out, L0_xattn_g_norm_in, L0_xattn_b_norm_in, L0_xattn_g_norm_out, L0_xattn_b_norm_out, L0_xattn_g_ffn, L0_xattn_b_ffn, L0_xattn_W1, L0_xattn_b1, L0_xattn_W2, L0_xattn_b2, L0_xattn_log_dt, L0_xattn_A_re, L0_xattn_A_im, L0_xattn_C_re, L0_xattn_C_im, L0_xattn_D_skip, L0_xattn_mod_gate, L0_attn_Wq, L0_attn_Wk, L0_attn_Wv, L0_attn_Wo, L0_ffn_gate_w, L0_ffn_w1, L0_ffn_w2):
    import jax
    import jax.numpy as jnp

    def _L0_xattn_ref(x_text, x_vision, text_mask, vision_mask, Wq, Wk, Wv, W_film_in, b_film_in, W_film_out, b_film_out, g_norm_in, b_norm_in, g_norm_out, b_norm_out, g_ffn, b_ffn, W1, b1, W2, b2, log_dt, A_re, A_im, C_re, C_im, D_skip, mod_gate):
        import jax, jax.numpy as jnp
        import numpy as np
        B, T, DT, G, DV = (16, 256, 512, 288, 384)
        H, DH = (4, 32)
        INNER = H * DH
        HID = 4 * DT
        N_STATE = 64
        K_TOP = 32

        def layernorm(x, g, b, eps=1e-05):
            m = x.mean(-1, keepdims=True)
            v = x.var(-1, keepdims=True)
            return (x - m) * jax.lax.rsqrt(v + eps) * g + b

        def s4d(x, log_dt, A_re, A_im, C_re, C_im, D_skip):
            Bb, L, D = x.shape
            dt = jnp.exp(log_dt)
            A = A_re + 1j * A_im
            C = C_re + 1j * C_im
            dtA = dt[:, None] * A
            dC = C * (jnp.exp(dtA) - 1.0) / A
            powers = jnp.exp(dtA[:, :, None] * jnp.arange(L))
            K = 2.0 * jnp.einsum('dn,dnl->dl', dC, powers).real
            n = 2 * L
            Kf = jnp.fft.rfft(K, n=n, axis=-1)
            xf = jnp.fft.rfft(x, n=n, axis=1)
            y = jnp.fft.irfft(xf * Kf.T[None], n=n, axis=1)[:, :L]
            return y + x * D_skip
        Bb, Tt, D = x_text.shape
        Gg = x_vision.shape[1]
        Q = (x_text @ Wq).reshape(Bb, Tt, H, DH)
        K = (x_vision @ Wk).reshape(Bb, Gg, H, DH)
        scores = jnp.einsum('bthd,bghd->bhtg', Q, K) / np.sqrt(DH).astype(np.float32)
        scores = jnp.where(vision_mask[:, None, None, :], scores, -jnp.inf)
        topv, topi = jax.lax.top_k(scores, K_TOP)
        probs = jax.nn.softmax(topv, axis=-1)
        bi = jnp.arange(Bb)[:, None, None, None]
        hi = jnp.arange(H)[None, :, None, None]
        ti = jnp.arange(Tt)[None, None, :, None]
        attn = jnp.zeros_like(scores).at[bi, hi, ti, topi].set(probs)
        attn_mean = attn.mean(axis=1)
        V = x_vision @ Wv
        c_t = jnp.einsum('btg,bgd->btd', attn_mean, V)
        c_t = c_t * text_mask[..., None]
        x = layernorm(x_text, g_norm_in, b_norm_in)
        scale_in, shift_in = jnp.split(c_t @ W_film_in + b_film_in, 2, axis=-1)
        x = x * (1.0 + mod_gate * scale_in) + mod_gate * shift_in
        y = s4d(x, log_dt, A_re, A_im, C_re, C_im, D_skip)
        scale_out, shift_out = jnp.split(c_t @ W_film_out + b_film_out, 2, axis=-1)
        y = y * (1.0 + mod_gate * scale_out) + mod_gate * shift_out
        xt = x_text + y
        h = layernorm(xt, g_ffn, b_ffn)
        h = jax.nn.gelu(h @ W1 + b1, approximate=False) @ W2 + b2
        xt = xt + h
        return layernorm(xt, g_norm_out, b_norm_out)

    def _L0_attn_ref(x, Wq, Wk, Wv, Wo):
        import jax, jax.numpy as jnp
        import numpy as np
        EMBED_DIM = 512
        NUM_HEADS = 16
        HEAD_DIM = EMBED_DIM // NUM_HEADS
        WINDOW_SIZE = 128
        SCALE = 1.0 / np.sqrt(HEAD_DIM)

        def _band_mask(T):
            i = jnp.arange(T)[:, None]
            j = jnp.arange(T)[None, :]
            full = j > i
            band = full & (j >= i - (WINDOW_SIZE - 1))
            return band
        B, T, C = x.shape
        H, D = (NUM_HEADS, HEAD_DIM)
        q = jnp.einsum('btc,oc->bto', x, Wq).reshape(B, T, H, D)
        k = jnp.einsum('btc,oc->bto', x, Wk).reshape(B, T, H, D)
        v = jnp.einsum('btc,oc->bto', x, Wv).reshape(B, T, H, D)
        att = jnp.einsum('bqhd,bkhd->bhqk', q, k) * SCALE
        mask = _band_mask(T)
        att = jnp.where(mask[None, None, :, :], -jnp.inf, att)
        att = jax.nn.softmax(att, axis=-1)
        out = jnp.einsum('bhqk,bkhd->bqhd', att, v).reshape(B, T, C)
        return jnp.einsum('btc,oc->bto', out, Wo)

    def _L0_ffn_ref(x, gate_w, w1, w2):
        import jax, jax.numpy as jnp
        import numpy as np
        D_MODEL = 512
        D_FF = 1024
        NUM_EXPERTS = 16
        TOP_K = 2
        CAPACITY_FACTOR = 1.25
        BATCH, SEQ = (4, 1024)
        B, S, d = x.shape
        T = B * S
        E, K = (NUM_EXPERTS, TOP_K)
        capacity = int(CAPACITY_FACTOR * T * K / E)
        xf = x.reshape(T, d)
        logits = xf @ gate_w.T
        probs = jax.nn.sigmoid(logits)
        top_vals, sel = jax.lax.top_k(probs, K)
        weights = top_vals / (top_vals.sum(-1, keepdims=True) + 1e-06)
        flat_sel = sel.reshape(-1)
        onehot = jax.nn.one_hot(flat_sel, E, dtype=jnp.int32)
        ranks = jnp.take_along_axis(jnp.cumsum(onehot, axis=0), flat_sel[:, None], axis=1)[:, 0] - 1
        valid = ranks < capacity
        sentinel = E * capacity
        slot = jnp.where(valid, flat_sel * capacity + ranks, sentinel)
        x_rep = jnp.repeat(xf, K, axis=0)
        padded = jnp.zeros((sentinel + 1, d), xf.dtype).at[slot].set(x_rep)
        padded = padded[:sentinel].reshape(E, capacity, d)
        h = jax.nn.gelu(jnp.einsum('ecd,edf->ecf', padded, w1), approximate=False)
        out_padded = jnp.einsum('ecf,efd->ecd', h, w2).reshape(sentinel, d)
        gathered = out_padded[jnp.minimum(slot, sentinel - 1)]
        gathered = jnp.where(valid[:, None], gathered, jnp.zeros((), xf.dtype))
        out = (gathered * weights.reshape(-1)[:, None]).reshape(T, K, d).sum(axis=1)
        return out.reshape(B, S, d)
    x = x + _L0_xattn_ref(_layernorm(x, axis=-1), ctx_768, mask_BxS_bf1, mask_BxS2_bf1, L0_xattn_Wq, L0_xattn_Wk, L0_xattn_Wv, L0_xattn_W_film_in, L0_xattn_b_film_in, L0_xattn_W_film_out, L0_xattn_b_film_out, L0_xattn_g_norm_in, L0_xattn_b_norm_in, L0_xattn_g_norm_out, L0_xattn_b_norm_out, L0_xattn_g_ffn, L0_xattn_b_ffn, L0_xattn_W1, L0_xattn_b1, L0_xattn_W2, L0_xattn_b2, L0_xattn_log_dt, L0_xattn_A_re, L0_xattn_A_im, L0_xattn_C_re, L0_xattn_C_im, L0_xattn_D_skip, L0_xattn_mod_gate)
    x = x + _L0_attn_ref(_layernorm(x, axis=-1), L0_attn_Wq, L0_attn_Wk, L0_attn_Wv, L0_attn_Wo)
    x = x + _L0_ffn_ref(_layernorm(x, axis=-1), L0_ffn_gate_w, L0_ffn_w1, L0_ffn_w2)
    return x

_drawn_inputs = setup_inputs


def setup_inputs(seed=0):
    import zlib

    import numpy as np

    out = dict(_drawn_inputs(seed))
    spreads = {'L0_xattn_b_film_in': (0.0, 0.1),
     'L0_xattn_b_film_out': (0.0, 0.1),
     'L0_xattn_g_norm_in': (1.0, 0.2),
     'L0_xattn_b_norm_in': (0.0, 0.1),
     'L0_xattn_g_norm_out': (1.0, 0.2),
     'L0_xattn_b_norm_out': (0.0, 0.1),
     'L0_xattn_g_ffn': (1.0, 0.2),
     'L0_xattn_b_ffn': (0.0, 0.336),
     'L0_xattn_b1': (0.0, 0.1),
     'L0_xattn_b2': (0.0, 0.1),
     'L0_xattn_A_re': (-0.5, 0.2)}
    factors = {}
    for name, (base, spread) in spreads.items():
        noise = np.random.default_rng([zlib.crc32(name.encode()), seed]).standard_normal(out[name].shape)
        drawn = base * np.exp(spread * noise) if base else spread * noise
        out[name] = jnp.asarray(drawn.astype(out[name].dtype))
    for name, factor in factors.items():
        out[name] = (out[name] * factor).astype(out[name].dtype)
    return out
```

```python
import math
from contextlib import ExitStack

import numpy as np
import concourse.bass as bass
from concourse import mybir

P = 128
B, T, D = 4, 128, 512
G, DV = 2048, 384
XH, DH = 4, 32
TOPK = 32
NCH = 32
NST = 64
HID = 4 * D
NH = 16
E, F, CAP = 16, 1024, 80
KD = D // P
KV = DV // P
GC, GT = G // 512, G // P
NT = B * XH
LA, LB = 8, 16
SCALE = 1.0 / math.sqrt(DH)
EPS = 1e-5
MASKED = -1.0e30
TAKEN = -3.0e38
ROUND = float(1.5 * 2 ** 23)
TWO_PI = 6.283185
NSLOT = E * CAP
CHUNK = (0, 5, 10, 16)
TR_X, TR_H, TR_A, TR_M = range(4)
N_LN = 6
VECS = ("g_in", "b_in", "g_ffn", "b_ffn", "g_out", "b_out", "b2")

CONST = {}
_at = 0
for _n, _w in [("ident", P), ("fxa", P), ("fxb", P), ("fkp", P), ("fkb", P), ("ga", P), ("gb", P),
               ("causal", P), ("tri", P), ("ones", P), ("diag", 16), ("slot", CAP), ("expert", E),
               ("first", E), ("lag_a", LA), ("lag_b", LB), ("off1", 1), ("off2", 1), ("sign", 1), ("mhalf", 4)]:
    CONST[_n] = (_at, _w)
    _at += _w
NCONST = _at


def shape_constants():
    c = np.zeros((P, NCONST), np.float32)

    def put(name, a):
        at, w = CONST[name]
        c[:, at:at + w] = a

    s = np.arange(P)[:, None].astype(np.float64)
    f = np.arange(P)[None, :].astype(np.float64)
    ang = 2 * np.pi * s * f / (2 * P)
    nyq = (-1.0) ** np.arange(P)
    put("ident", np.eye(P))
    put("fxa", np.cos(ang))
    fxb = -np.sin(ang)
    put("fkb", fxb)
    fxb = fxb.copy(); fxb[:, 0] = nyq
    put("fxb", fxb)
    fkp = np.cos(ang); fkp[:, 0] = nyq
    put("fkp", fkp)
    w = np.where(np.arange(P) == 0, 1.0, 2.0)[:, None] / (2 * P)
    put("ga", w * np.cos(ang.T))
    gb = -w * np.sin(ang.T)
    gb[0, :] = nyq / (2 * P)
    put("gb", gb)
    q = np.arange(P)
    put("causal", np.where(q[None, :] > q[:, None], MASKED, 0.0))
    put("tri", (q[:, None] < q[None, :]).astype(float))
    put("ones", 1.0)
    row_d = q % 16
    col_d = np.arange(16)
    put("diag", (row_d[:, None] == col_d[None, :]).astype(float))
    put("slot", np.arange(CAP)[None, :])
    put("expert", np.arange(E)[None, :])
    put("first", CAP * np.arange(E)[None, :])
    put("lag_a", LB * np.arange(LA)[None, :])
    put("lag_b", np.arange(LB)[None, :])
    top = (q < NST).astype(float)[:, None]
    put("off1", 0.25 * top)
    put("off2", 0.25 * (1 - top))
    put("sign", 2 * top - 1)
    put("mhalf", -0.5)
    return c


def build(nc, I, out, yrows, kdram):
    fp32, bf16, u32, u8 = mybir.dt.float32, mybir.dt.bfloat16, mybir.dt.uint32, mybir.dt.uint8
    ALU, ACT, AX = mybir.AluOpType, mybir.ActivationFunctionType, mybir.AxisListType
    ctx = ExitStack()
    with ctx:
        def sb(name, shape, dt=fp32):
            return ctx.enter_context(nc.sbuf_tensor(name, shape, dt))

        class Sems(dict):
            def __missing__(self, name):
                self[name] = ctx.enter_context(nc.semaphore(name))
                return self[name]

        S_ = Sems()

        X = sb("X", [P, B, D])
        XT = sb("XT", [P, B, D])
        TT = sb("TT", [P, KD, D])
        QT = sb("QT", [P, B * T])
        CST = sb("CST", [P, NCONST])
        KA = sb("KA", [P, D])
        KP = sb("KP", [P, D])
        KB = sb("KB", [P, D])
        WQ = sb("WQ", [P, KD, P])
        WK = sb("WK", [P, KV, P])
        CCT = sb("CCT", [P, KV, B * T])
        CC = sb("CC", [P, DV])
        MU8 = sb("MU8", [P, G], u8)
        MROW = sb("MROW", [P, G], bf16)
        ONEB = sb("ONEB", [P, P], bf16)
        V32 = sb("V32", [P, 2, TOPK])
        V33 = sb("V33", [P, 8])
        TH = sb("TH", [P, 2])
        C8 = sb("C8", [P, 1])
        FL = sb("FL", [P, 1])
        FQ = sb("FQ", [32, 4])
        FT = sb("FT", [32, 32])
        FTT = sb("FTT", [32, 32])
        FM = sb("FM", [1, 1], u32)
        EV = sb("EV", [P, TOPK])
        SM = sb("SM", [P, 2, 4])
        BN = sb("BN", [P, B, 6])
        MV = sb("MV", [P, B, 2])
        VE = sb("VE", [P, B])
        RS = sb("RS", [P, B])
        TM8 = sb("TM8", [P, B], u8)
        TM = sb("TM", [P, B])
        MG = sb("MG", [P, 1])
        DSK = sb("DSK", [P, KD])
        B1 = sb("B1", [P, HID // P])
        PR = sb("PR", [P, B, E])
        V8 = sb("V8", [P, B, 8])
        I8 = sb("I8", [P, B, 8], u32)
        I8F = sb("I8F", [P, B, 2])
        OH = sb("OH", [P, B, 2, E])
        PICK = sb("PICK", [P, B, E])
        RK = sb("RK", [P, B, E])
        RT = sb("RT", [P, B, E])
        R2 = sb("R2", [P, B, 2])
        SL = sb("SL", [P, B, 2])
        SLU = sb("SLU", [P, B, 2], u32)
        WT2 = sb("WT2", [P, B, 2])
        WS = sb("WS", [P, B, 4])
        EV3 = sb("EV3", [P, 1])
        GWT = sb("GWT", [P, KD, E])

        AR_W = 37888
        AR = sb("AR", [P, AR_W])

        def at(off, *shape):
            n = int(np.prod(shape))
            assert off + n <= AR_W
            v = AR[:, off:off + n]
            if len(shape) == 2:
                v = v.rearrange("p (a b) -> p a b", b=shape[1])
            elif len(shape) == 3:
                v = v.rearrange("p (a b c) -> p a b c", b=shape[1], c=shape[2])
            return v

        CTX = at(0, GT, DV)
        CXT = at(6144, KV, G)
        KT = at(13824, G)
        SC = [at(15872, G), at(17920, G)]
        W = [at(19968, G), at(22016, G)]
        DS = at(24064, G)
        AT = at(26112, GT, P)
        ABC = at(19968, 4, D)
        ZT = at(28160, LB, P)
        MGN = at(30208, LB, P)
        PM = at(32256, P // 16, LA, 16)
        PW = at(33280, P // 16, LA, 16)
        SA = [at(28160 + 512 * n, D) for n in range(12)]
        AL, UT, A1, A2 = (at(34304 + 512 * n, D) for n in range(4))
        CAND = [at(36352, NCH, 8), at(36608, NCH, 8)]
        RD = at(36864, 32, LB)
        GD = at(37376, D)
        KRAW = QT[:, :].rearrange("p (a b) -> p a b", b=P)
        KTD, DTE, RDEN = KA, KA, KP
        WV = at(12288, KV, D)
        WFI, WFO = at(6144, KD, 2 * D), at(0, KD, 2 * D)
        U = [at(4096 + 512 * n, D) for n in range(4)]
        GEL = at(0, HID // P, B * T)
        XL = at(13824, B, D)
        VEC = {n: at(15872 + 512 * k, D) for k, n in enumerate(VECS)}
        BFI, BFO = at(19456, 2, D), at(20480, 2, D)
        W1 = at(21504, KD, HID)
        W2 = at(29696, HID // P, D)
        WTR = at(21504, 4, KD, D)
        QA, KS, VA = at(29696, KD, B * T), at(31744, KD, B * T), at(33792, B, D)
        PB = [at(35840 + 512 * n, B, T) for n in range(3)]
        PBT = [at(13824, B, T), at(14336, B, T)]
        ONEH = at(15872, B, E, CAP)
        XET = at(21504, KD, NSLOT)
        Y = [at(26624, D), at(27136, D)]
        H = [at(8192, F), at(9216, F)]
        HT = [at(10240, F // P, CAP), at(10880, F // P, CAP)]
        GA = at(15872, B, 2, D)
        EW1 = [at(0, KD, F), at(29696, KD, F)]
        EW2 = [at(4096, F // P, D), at(33792, F // P, D)]

        def c(name, rows=P):
            o, w = CONST[name]
            return CST[0:rows, o:o + w]

        ident = c("ident")
        PS = ctx.enter_context(nc.psum_tensor("PS", [P, 8, 512], fp32))
        block = ctx.enter_context(nc.Block())

        class Chain:

            def __init__(self, eng, name):
                self.eng, self.sem, self.n = eng, S_[name], 0

            def __call__(self, ins):
                self.n += 1
                ins.then_inc(self.sem, 1)
                self.eng.wait_ge(self.sem, self.n)

        @block.sync
        def _(eng):
            def load(dst, src, sem):
                eng.dma_start(dst, src).then_inc(S_[sem], 16)

            load(X[:, :, :], I["x"].rearrange("b t d -> t b d"), "ld_x")
            load(CST[:, :], I["consts"], "ld_c")
            load(WQ[:, :, :], I["Wq"].rearrange("(k p) n -> p k n", p=P), "ld_w")
            load(WK[:, :, :], I["Wk"].rearrange("(k p) n -> p k n", p=P), "ld_w")
            ctxv = I["ctx"].rearrange("b (j p) d -> b p j d", p=P)
            cxtv = I["ctxT"].rearrange("b (j p) g -> b p j g", p=P)

            def load_ctxT(b):
                for k in range(GC):
                    cols = slice(k * 512, k * 512 + 512)
                    load(CXT[:, :, cols], cxtv[b, :, :, cols], f"ld_cxt{k}")

            def load_ctx(b):
                for k in range(GC):
                    load(CTX[:, 4 * k:4 * k + 4, :], ctxv[b, :, 4 * k:4 * k + 4, :], f"ld_ctx{k}")

            def load_mask(b):
                load(MU8[:, :], I["mask_ctx"][b, :].partition_broadcast(P), "ld_mask")

            load_ctxT(0)
            load_mask(0)
            for n, a in enumerate(("A_re", "A_im", "C_re", "C_im")):
                for half in (0, NST):
                    load(ABC[half:half + NST, n, :], I[a], "ld_raw")
            load(DTE[:, :], I["log_dt"].partition_broadcast(P), "ld_dt")
            load(TM8[:, :], I["mask_x"], "ld_small")
            load(MG[:, :], I["mod_gate"].partition_broadcast(P), "ld_small")
            load(DSK[:, :], I["D_skip"], "ld_small")
            load(B1[:, :], I["b1"], "ld_small")
            load(GWT[:, :, :], I["gate_w"].rearrange("(k p) e -> p k e", p=P), "ld_small")
            load_ctx(0)
            load(WV[:, :, :], I["Wv"].rearrange("(k p) n -> p k n", p=P), "ld_wv")
            for b in range(1, B):
                eng.wait_ge(S_["kt_ps"], GC * b)
                load_ctxT(b)
                eng.wait_ge(S_["mask_row"], b)
                load_mask(b)
                eng.wait_ge(S_["cc_ps"], b)
                load_ctx(b)
            eng.wait_ge(S_["kt_ps"], GC * B)
            load(WFI[:, :, :], I["W_film_in"].rearrange("(k p) n -> p k n", p=P), "ld_wfi")
            kv = kdram.rearrange("(g d) (a m) -> a d g m", d=16, m=LB)
            eng.wait_ge(S_["diag"], 16)
            for a in range(LA):
                eng.dma_start(kv[a], RD[16 * a:16 * a + 16, :, :]).then_inc(S_["st_k"], 16)
            eng.wait_ge(S_["st_k"], 16 * LA)
            eng.wait_ge(S_["s_ps"], GC * NT)
            load(KRAW, kdram.rearrange("(k p) l -> p k l", p=P), "ld_k")
            eng.wait_ge(S_["cc_ps"], B)
            load(WFO[:, :, :], I["W_film_out"].rearrange("(k p) n -> p k n", p=P), "ld_wfo")
            eng.wait_ge(S_["d_done"], NT)
            for n in VECS:
                load(VEC[n], I[n].partition_broadcast(P), "ld_vec")
            load(BFI.rearrange("p a b -> p (a b)"), I["b_film_in"].partition_broadcast(P), "ld_vec")
            load(BFO.rearrange("p a b -> p (a b)"), I["b_film_out"].partition_broadcast(P), "ld_vec")
            eng.wait_ge(S_["g_ps"], 16)
            load(W1[:, :, :], I["W1"].rearrange("(k p) n -> p k n", p=P), "ld_w1")
            load(W2[:, :, :], I["W2"].rearrange("(k p) n -> p k n", p=P), "ld_w2")
            eng.wait_ge(S_["f1_ps"], HID // P)
            for n, a in enumerate(("Aq", "Ak", "Av", "Ao")):
                load(WTR[:, n, :, :], I[a].rearrange("(k p) n -> p k n", p=P), f"ld_attn{n}")
            w1v = I["w1"].rearrange("e (k p) n -> e p k n", p=P)
            w2v = I["w2"].rearrange("e (k p) n -> e p k n", p=P)

            def load_w1(e):
                load(EW1[e % 2][:, :, :], w1v[e], f"ld_e1{e % 2}")

            def load_w2(e):
                load(EW2[e % 2][:, :, :], w2v[e], f"ld_e2{e % 2}")

            eng.wait_ge(S_["f2_ps"], B)
            load_w1(0)
            load_w2(0)
            eng.wait_ge(S_["av_ps"], NH)
            load_w1(1)
            load_w2(1)
            for e in range(2, E):
                eng.wait_ge(S_["m1_ps"], e - 1)
                load_w1(e)
                eng.wait_ge(S_["m2_ps"], e - 1)
                load_w2(e)
            for b in range(B):
                eng.wait_ge(S_["fin"], b + 1)
                eng.dma_start(out[b], X[:, b, :]).then_inc(S_["st_out"], 16)
            eng.wait_ge(S_["st_out"], 16 * B)

        @block.gpsimd
        def _(eng):
            link = Chain(eng, "pool_chain")

            def rstd(n):
                eng.wait_ge(S_["var"], n)
                eng.tensor_tensor(RS[:, :], VE[:, :], c("mhalf"), ALU.pow).then_inc(S_["rstd"], 1)

            def mask_row(b):
                eng.wait_ge(S_["ld_mask"], 16 * (b + 1))
                if b:
                    eng.wait_ge(S_["s_ps"], GC * XH * b)
                eng.tensor_scalar(MROW[:, :], MU8[:, :], -MASKED, MASKED, ALU.mult, ALU.add)\
                   .then_inc(S_["mask_row"], 1)

            def add_head(i):
                b, h = divmod(i, XH)
                eng.wait_ge(S_["masked"], i + 1)
                w = W[i % 2]
                if h == 0:
                    if b:
                        eng.wait_ge(S_["at_ps"], 4 * b)
                    eng.tensor_scalar(DS, w, 1.0, None, ALU.mult).then_inc(S_["d_done"], 1)
                else:
                    eng.wait_ge(S_["d_done"], i)
                    eng.tensor_tensor(DS, DS, w, ALU.add).then_inc(S_["d_done"], 1)

            def fraction(n, turn):
                t, r = ZT[:, 0:n, :], MGN[:, 0:n, :]
                eng.wait_ge(S_["turn"], turn)
                link(eng.tensor_scalar(r, t, ROUND, -ROUND, ALU.add, ALU.add))
                eng.tensor_tensor(t, t, r, ALU.subtract).then_inc(S_["frac"], 1)

            def piece(i):
                q, k = divmod(i, 4)
                if k == 0:
                    fraction(LA, 2 * q + 1)
                if k == 1:
                    eng.wait_ge(S_["trig"], 2 * q + 1)
                    by_lag = lambda v: v.rearrange("p a (g m) -> p a g m", m=16)
                    eng.tensor_tensor(PM.rearrange("p g a m -> p a g m"), by_lag(ZT[:, 0:LA, :]),
                                      by_lag(MGN[:, 0:LA, :]), ALU.mult).then_inc(S_["pm_read"], 1)
                    eng.wait_ge(S_["pm_read"], q + 1)
                    for lo, hi in ((0, NST), (NST, 0)):
                        eng.dma_start(PW[hi:hi + NST], PM[lo:lo + NST]).then_inc(S_["swap"], 16)
                    eng.wait_ge(S_["swap"], 32 * (q + 1))
                    a1, a2 = (v[:, q * P:(q + 1) * P].rearrange("p (g m) -> p g m", m=16).unsqueeze(2)
                              .broadcast_to([P, P // 16, LA, 16]) for v in (A1, A2))
                    link(eng.tensor_tensor(PM, PM, a1, ALU.mult))
                    link(eng.tensor_tensor(PW, PW, a2, ALU.mult))
                    link(eng.tensor_tensor(PM, PM, PW, ALU.add))
                if k == 2:
                    fraction(LB, 2 * q + 2)
                if k == 3:
                    eng.wait_ge(S_["trig"], 2 * q + 2)
                    eng.tensor_tensor(ZT, ZT, MGN, ALU.mult).then_inc(S_["powers"], 1)

            link(eng.memset(ONEB[:, :], 1.0))
            eng.wait_ge(S_["ld_c"], 16)
            rstd(1)
            mask_row(0)
            for i in range(NT + 1):
                if i:
                    add_head(i - 1)
                if i < NT:
                    if i % 4 == 2 and i // 4 + 1 < B:
                        mask_row(i // 4 + 1)
                    piece(i)
            for n in range(2, N_LN + 1):
                rstd(n)
            eng.wait_ge(S_["slots"], 1)
            for k in range(2):
                eng.wait_ge(S_[f"st_y{k}"], 16 * E // 2)
            for b in range(B):
                for k in range(2):
                    eng.indirect_dma_start(GA[:, b, k, :], None, yrows, bass.IndirectOffsetOnAxis(
                        ap=SLU[:, b, k:k + 1], axis=0)).then_inc(S_["ld_g"], 16)

        @block.scalar
        def _(eng):
            link = Chain(eng, "act_chain")

            def evac_transposed(n, dst, first=0):
                eng.wait_ge(S_["tr_ps"], n + 1)
                for k in range(4):
                    eng.activation(dst[:, k, :], PS[:, first + k, :], ACT.Copy).then_inc(S_["tr_sb"], 1)

            def context_keys(b):
                for k in range(GC):
                    eng.wait_ge(S_["kt_ps"], b * GC + k + 1)
                    if k == 0 and b:
                        eng.wait_ge(S_["s_ps"], GC * XH * b)
                    eng.activation(KT[:, k * 512:(k + 1) * 512], PS[:, 3, :], ACT.Copy)\
                       .then_inc(S_["kt_sb"], 1)

            def scores(i):
                if i >= 2:
                    eng.wait_ge(S_["masked"], i - 1)
                for k in range(GC):
                    eng.wait_ge(S_["s_ps"], GC * i + k + 1)
                    eng.activation(SC[i % 2][:, k * 512:(k + 1) * 512], PS[:, 4 + k % 2, :], ACT.Copy)\
                       .then_inc(S_["s_sb"], 1)

            def exponentials(i):
                v, m = V32[:, i % 2, :], SM[:, i % 2, :]
                eng.wait_ge(S_["topk"], i + 1)
                link(eng.activation(m[:, 0:1], v[:, 0:1], ACT.Copy, scale=-SCALE))
                link(eng.activation(EV[:, :], v, ACT.Exp, bias=m[:, 0:1], scale=SCALE, accum_out=m[:, 1:2]))
                link(eng.activation(m[:, 2:3], m[:, 1:2], ACT.Ln, scale=float(XH)))
                link(eng.activation(m[:, 3:4], m[:, 2:3], ACT.Identity, bias=m[:, 0:1], scale=-1.0))
                if i >= 2:
                    eng.wait_ge(S_["d_done"], i - 1)
                eng.activation(W[i % 2], SC[i % 2], ACT.Exp, bias=m[:, 3:4], scale=SCALE)\
                   .then_inc(S_["e_done"], 1)

            def attended(b):
                for k in range(4):
                    eng.wait_ge(S_["at_ps"], 4 * b + k + 1)
                    if b and k == 0:
                        eng.wait_ge(S_["cc_ps"], b)
                    eng.activation(AT[:, 4 * k:4 * k + 4, :], PS[:, 6 + k % 2, :]
                                   .rearrange("p (a b) -> p a b", b=P), ACT.Copy).then_inc(S_["at_sb"], 1)
                eng.wait_ge(S_["cc_ps"], b + 1)
                eng.wait_ge(S_["tmask"], 1)
                eng.activation(CC[:, :], PS[:, 3, 0:DV], ACT.Copy, scale=TM[:, b:b + 1]).then_inc(S_["cc_sb"], 1)
                eng.wait_ge(S_["cct_ps"], b + 1)
                eng.activation(CCT[:, :, b * T:(b + 1) * T], PS[:, 3, 0:DV].rearrange("p (a b) -> p a b", b=P),
                               ACT.Copy).then_inc(S_["cct_sb"], 1)

            def turns(q, n, step):
                if q == 0 and step == LB:
                    eng.wait_ge(S_["coef"], 1)
                if q and step == LB:
                    eng.wait_ge(S_["g_ps"], 4 * q)
                if step == 1:
                    eng.wait_ge(S_["pm_read"], q + 1)
                for k in range(n):
                    last = eng.activation(ZT[:, k, :], UT[:, q * P:(q + 1) * P], ACT.Identity,
                                          bias=c("off1"), scale=float(step * k))
                last.then_inc(S_["turn"], 1)

            def powers(q, n, step):
                al = AL[:, q * P:(q + 1) * P]
                link(eng.activation(ZT[:, 0:n, :], ZT[:, 0:n, :], ACT.Sin, scale=TWO_PI))
                for k in range(n):
                    last = eng.activation(MGN[:, k, :], al, ACT.Exp, scale=float(step * k))
                last.then_inc(S_["trig"], 1)

            def piece(i):
                q, k = divmod(i, 4)
                if k == 0:
                    turns(q, LA, LB)
                if k == 1:
                    eng.wait_ge(S_["frac"], 2 * q + 1)
                    powers(q, LA, LB)
                if k == 2:
                    turns(q, LB, 1)
                if k == 3:
                    eng.wait_ge(S_["frac"], 2 * q + 2)
                    powers(q, LB, 1)

            evac_transposed(TR_X, TT)
            eng.wait_ge(S_["q_ps"], 1)
            eng.activation(QT[:, :], PS[:, 4, :], ACT.Copy).then_inc(S_["q_sb"], 1)
            eng.wait_ge(S_["ld_dt"], 16)
            eng.activation(DTE[:, :], DTE[:, :], ACT.Exp).then_inc(S_["dt"], 1)
            context_keys(0)
            eng.wait_ge(S_["phase"], 1)
            eng.activation(SA[4], AL, ACT.Tanh, scale=0.5).then_inc(S_["s4"], 1)
            eng.activation(SA[5], AL, ACT.Exp).then_inc(S_["s4"], 1)
            eng.activation(SA[2], SA[2], ACT.Sin, scale=TWO_PI).then_inc(S_["s4"], 1)
            eng.activation(SA[3], SA[3], ACT.Sin, scale=TWO_PI).then_inc(S_["s4"], 1)
            scores(0)
            scores(1)
            for i in range(NT + 1):
                if i:
                    exponentials(i - 1)
                if i and i % 4 == 0:
                    attended(i // 4 - 1)
                if 1 <= i < NT - 1 + 1 and i + 1 < NT:
                    scores(i + 1)
                if i < NT:
                    piece(i)
                if i % 4 == 2 and i // 4 + 1 < B:
                    context_keys(i // 4 + 1)
            eng.wait_ge(S_["kt2_ps"], 1)
            eng.activation(KTD[:, :], PS[:, 0, :], ACT.Copy).then_inc(S_["ktd"], 1)
            eng.wait_ge(S_["spec_ps"], 1)
            for n, dst in enumerate((KA, KP, KB)):
                eng.activation(dst[:, :], PS[:, 1 + n, :], ACT.Copy).then_inc(S_["spec"], 1)
            eng.wait_ge(S_["ct_ps"], 1)
            for k in range(KD):
                eng.activation(TT[:, k, :], PS[:, 4 + k, :], ACT.Copy).then_inc(S_["ct_sb"], 1)
            evac_transposed(TR_H, TT)
            eng.wait_ge(S_["x3"], B)
            for f in range(HID // P):
                eng.wait_ge(S_["f1_ps"], f + 1)
                eng.activation(GEL[:, f, :], PS[:, 4 + f % 4, :], ACT.Gelu, bias=B1[:, f:f + 1])\
                   .then_inc(S_["gelu"], 1)
            evac_transposed(TR_A, TT)
            for n in range(12):
                eng.wait_ge(S_["qkv_ps"], n + 1)
                dst = (QA, KS, VA)[n // 4]
                eng.activation(dst[:, n % 4, :], PS[:, 4 + n % 4, :], ACT.Copy).then_inc(S_["qkv_sb"], 1)
            for u in range(NH + 1):
                if u < NH:
                    eng.wait_ge(S_["a_shift"], u + 1)
                    eng.activation(PB[u % 3], PB[u % 3], ACT.Exp).then_inc(S_["a_exp"], 1)
                if u:
                    v = u - 1
                    eng.wait_ge(S_["pt_ps"], v + 1)
                    if v >= 2:
                        eng.wait_ge(S_["av_ps"], v - 1)
                    eng.activation(PBT[v % 2], PS[:, 6 + v % 2, :].rearrange("p (a b) -> p a b", b=P),
                                   ACT.Copy).then_inc(S_["pt_sb"], 1)
                    if v % 4 == 3:
                        eng.wait_ge(S_["av_ps"], v + 1)
                        eng.activation(TT[:, v // 4, :], PS[:, v // 4, :], ACT.Copy).then_inc(S_["ao_sb"], 1)
            evac_transposed(TR_M, TT)
            eng.wait_ge(S_["lg_ps"], 1)
            eng.activation(PR[:, :, :], PS[:, 5, 0:B * E].rearrange("p (a b) -> p a b", b=E),
                           ACT.Sigmoid).then_inc(S_["probs"], 1)
            for n in range(12):
                k, ch = n % 4, n // 4
                eng.wait_ge(S_["xe_ps"], n + 1)
                eng.activation(XET[:, k, CHUNK[ch] * CAP:CHUNK[ch + 1] * CAP],
                               PS[:, k, 0:(CHUNK[ch + 1] - CHUNK[ch]) * CAP], ACT.Copy).then_inc(S_["xe_sb"], 1)
            for e in range(E + 1):
                if e < E:
                    eng.wait_ge(S_["m1_ps"], e + 1)
                    if e >= 2:
                        eng.wait_ge(S_["ht_ps"], 2 * (e - 1))
                    for j in range(2):
                        eng.activation(H[e % 2][0:CAP, 512 * j:512 * j + 512], PS[0:CAP, 4 + j, :], ACT.Gelu)\
                           .then_inc(S_["h_sb"], 1)
                if e:
                    v = e - 1
                    eng.wait_ge(S_["m2_ps"], v + 1)
                    if v >= 2:
                        eng.wait_ge(S_[f"st_y{v % 2}"], 16 * (v // 2))
                    eng.activation(Y[v % 2][0:CAP, :], PS[0:CAP, v % 2, :], ACT.Copy).then_inc(S_["y_sb"], 1)
                    eng.wait_ge(S_["y_sb"], v + 1)
                    eng.dma_start(yrows[v * CAP:(v + 1) * CAP, :], Y[v % 2][0:CAP, :]).then_inc(S_[f"st_y{v % 2}"], 16)

        @block.vector
        def _(eng):
            link = Chain(eng, "dve_chain")
            exact_link = Chain(eng, "exact_chain")
            count = [0]

            def layernorm(src, dst, gain=None, bias=None, done=None):
                count[0] += 1
                for b in range(B):
                    link(eng.bn_stats(out=BN[:, b, :], in_=src[:, b, :]))
                for b in range(B):
                    link(eng.bn_aggr(out=MV[:, b, :], in_=BN[:, b, :]))
                eng.tensor_scalar(VE[:, :], MV[:, :, 1], EPS, None, ALU.add).then_inc(S_["var"], 1)
                eng.wait_ge(S_["rstd"], count[0])
                for b in range(B):
                    last = eng.tensor_scalar(dst[:, b, :], src[:, b, :], MV[:, b, 0:1], RS[:, b:b + 1],
                                             ALU.subtract, ALU.mult)
                    if gain is not None:
                        link(last)
                        link(eng.tensor_tensor(dst[:, b, :], dst[:, b, :], gain, ALU.mult))
                        last = eng.tensor_tensor(dst[:, b, :], dst[:, b, :], bias, ALU.add)
                    if done:
                        last.then_inc(S_[done], 1)
                    else:
                        link(last)

            def exact(i):
                s, w, v = SC[i % 2], W[i % 2], V32[:, i % 2, :]
                n0 = exact_link.n
                for r in range(TOPK // 8):
                    src = s if r == 0 else w
                    exact_link(eng.max(v[:, 8 * r:8 * r + 8], src))
                    exact_link(eng.match_replace(out=w, in_to_replace=v[:, 8 * r:8 * r + 8], in_values=src,
                                                 imm_value=TAKEN))
                exact_link(eng.tensor_scalar(w, w, TAKEN, None, ALU.is_equal))
                exact_link(eng.tensor_scalar(w, w, -TAKEN, TAKEN, ALU.mult, ALU.add))
                exact_link(eng.tensor_tensor(s, s, w, ALU.add))
                exact_link(eng.memset(TH[:, i % 2:i % 2 + 1], TAKEN / 10))
                return exact_link.n - n0

            def topk(i):
                s, v = SC[i % 2], V32[:, i % 2, :]
                per = 512 * NCH // G
                for k in range(GC):
                    eng.wait_ge(S_["s_sb"], GC * i + k + 1)
                    for n in range(per * k, per * (k + 1)):
                        last = eng.max(CAND[0][:, n, :], s[:, n * G // NCH:(n + 1) * G // NCH])
                link(last)
                if i:
                    masked(i - 1)
                if i >= 2:
                    eng.wait_ge(S_["e_done"], i - 1)
                flat = [x.rearrange("p a b -> p (a b)") for x in CAND]
                for r in range(TOPK // 8):
                    src = flat[min(r, 1)]
                    link(eng.max(v[:, 8 * r:8 * r + 8], src))
                    link(eng.match_replace(out=flat[1], in_to_replace=v[:, 8 * r:8 * r + 8], in_values=src,
                                           imm_value=TAKEN))
                link(eng.max(V33[:, :], flat[1]))
                link(eng.reduce_max(C8[:, :], CAND[0][:, :, 7], AX.X))
                link(eng.tensor_copy(TH[:, i % 2:i % 2 + 1], v[:, TOPK - 1:TOPK]))
                link(eng.scalar_tensor_tensor(out=FL[:, :], in0=C8[:, :], scalar=V33[:, 0:1],
                                              in1=v[:, TOPK - 1:TOPK], op0=ALU.max, op1=ALU.is_ge))
                for g in range(4):
                    last = eng.tensor_copy(FQ[:, g:g + 1], FL[32 * g:32 * g + 32, :])
                link(last)
                link(eng.reduce_max(FT[:, 0:1], FQ[:, :], AX.X))
                link(eng.transpose(FTT[:, :], FT[:, :]))
                link(eng.reduce_max(FM[0:1, :], FTT[0:1, :], AX.X))
                if i >= 2:
                    eng.wait_ge(S_["d_done"], i - 1)
                unsettled = eng.value_load(FM[0:1, 0:1], min_val=0, max_val=1)
                with eng.If(unsettled > 0):
                    n = exact(i)
                with eng.Else():
                    eng.sem_inc(S_["exact_chain"], n)
                eng.memset(EV3[:, :], 0.0).then_inc(S_["topk"], 1)

            def masked(i):
                eng.wait_ge(S_["e_done"], i + 1)
                eng.scalar_tensor_tensor(out=W[i % 2], in0=SC[i % 2], scalar=TH[:, i % 2:i % 2 + 1], in1=W[i % 2],
                                         op0=ALU.is_ge, op1=ALU.mult).then_inc(S_["masked"], 1)

            def diagonal(q):
                for j in range(4):
                    eng.wait_ge(S_["g_ps"], 4 * q + j + 1)
                    m = c("diag").unsqueeze(1).broadcast_to([P, 2 * LB, 16])
                    link(eng.tensor_tensor(GD.rearrange("p (a b) -> p a b", b=16),
                                           PS[:, 6 + j % 2, :].rearrange("p (a b) -> p a b", b=16), m, ALU.mult))
                    g = 8 * q + 2 * j
                    link(eng.reduce_sum(RD[:, g:g + 2, :],
                                        GD.rearrange("p (a b c) -> p a b c", b=LB, c=16), AX.X))
                    eng.memset(EV3[:, :], 0.0).then_inc(S_["diag"], 1)

            eng.wait_ge(S_["ld_x"], 16)
            layernorm(X, XT, done="xt")
            eng.wait_ge(S_["ld_raw"], 16 * 8)
            eng.wait_ge(S_["dt"], 1)
            are, aim, cr, ci = (ABC[:, n, :] for n in range(4))
            tt, ts = eng.tensor_tensor, eng.tensor_scalar
            mul, add, sub = ALU.mult, ALU.add, ALU.subtract
            link(tt(AL, DTE[:, :], are, mul))
            link(tt(UT, DTE[:, :], aim, mul))
            link(ts(UT, UT, 1.0 / (2 * math.pi), None, mul))
            link(ts(SA[0], UT, 0.5, None, mul))
            link(ts(SA[1], SA[0], ROUND, -ROUND, add, add))
            link(tt(SA[2], SA[0], SA[1], sub))
            link(ts(SA[1], UT, ROUND, -ROUND, add, add))
            tt(SA[3], UT, SA[1], sub).then_inc(S_["phase"], 1)
            link(tt(RDEN[:, :], are, are, mul))
            link(tt(SA[6], aim, aim, mul))
            link(tt(RDEN[:, :], RDEN[:, :], SA[6], add))
            link(eng.reciprocal(RDEN[:, :], RDEN[:, :]))
            eng.wait_ge(S_["s4"], 4)
            link(eng.scalar_tensor_tensor(out=SA[4], in0=SA[5], scalar=1.0, in1=SA[4], op0=add, op1=mul))
            link(tt(SA[2], SA[2], SA[2], mul))
            link(ts(SA[2], SA[2], -2.0, None, mul))
            link(tt(SA[6], SA[4], SA[2], mul))
            link(tt(SA[6], SA[6], SA[4], add))
            link(tt(SA[6], SA[6], SA[2], add))
            link(tt(SA[7], SA[5], SA[3], mul))
            link(tt(SA[8], cr, SA[6], mul))
            link(tt(SA[9], ci, SA[7], mul))
            link(tt(SA[8], SA[8], SA[9], sub))
            link(tt(SA[9], cr, SA[7], mul))
            link(tt(SA[10], ci, SA[6], mul))
            link(tt(SA[9], SA[9], SA[10], add))
            link(tt(SA[10], SA[8], are, mul))
            link(tt(SA[11], SA[9], aim, mul))
            link(tt(SA[10], SA[10], SA[11], add))
            link(tt(SA[10], SA[10], RDEN[:, :], mul))
            link(tt(SA[11], SA[9], are, mul))
            link(tt(SA[9], SA[8], aim, mul))
            link(tt(SA[11], SA[11], SA[9], sub))
            link(tt(SA[11], SA[11], RDEN[:, :], mul))
            link(ts(A1, SA[10], c("sign"), 2.0, mul, mul))
            ts(A2, SA[11], -2.0, None, mul).then_inc(S_["coef"], 1)
            eng.wait_ge(S_["ld_small"], 16 * 5)
            eng.tensor_copy(TM[:, :], TM8[:, :]).then_inc(S_["tmask"], 1)
            link(eng.memset(FT[:, :], 0.0))
            for i in range(NT):
                topk(i)
                if i and i % 4 == 0:
                    diagonal(i // 4 - 1)
            masked(NT - 1)
            diagonal(3)
            eng.wait_ge(S_["ld_k"], 16)
            tt(KRAW[:, :, 0], KRAW[:, :, 0], DSK[:, :], add).then_inc(S_["kraw"], 1)
            eng.wait_ge(S_["d_done"], NT)
            eng.wait_ge(S_["ld_vec"], 16 * (len(VECS) + 2))
            layernorm(XT, XL, VEC["g_in"], VEC["b_in"])
            for v in (BFI, BFO):
                link(ts(v[:, 0, :], v[:, 0, :], MG[:, 0:1], 1.0, mul, add))
                link(ts(v[:, 1, :], v[:, 1, :], MG[:, 0:1], None, mul))
            eng.wait_ge(S_["spec"], 3)

            def film(dst, ps, bias):
                return eng.scalar_tensor_tensor(out=dst, in0=ps, scalar=MG[:, 0:1], in1=bias, op0=mul, op1=add)

            def modulate(b):
                xl = XL[:, b, :]
                eng.wait_ge(S_["fi_ps"], b + 1)
                link(film(U[1], PS[:, 4, :], BFI[:, 0, :]))
                link(tt(xl, xl, U[1], mul))
                link(film(U[1], PS[:, 5, :], BFI[:, 1, :]))
                link(tt(xl, xl, U[1], add))
                eng.memset(EV3[:, :], 0.0).then_inc(S_["x2"], 1)

            modulate(0)
            for b in range(B):
                eng.wait_ge(S_["xf_ps"], b + 1)
                link(tt(U[0], PS[:, 0, :], KA[:, :], mul))
                link(tt(U[1], PS[:, 1, :], KB[:, :], mul))
                link(tt(U[0], U[0], U[1], sub))
                link(tt(U[2], PS[:, 0, :], KB[:, :], mul))
                link(tt(U[3], PS[:, 1, :], KP[:, :], mul))
                tt(U[2], U[2], U[3], add).then_inc(S_["yf"], 1)
                eng.wait_ge(S_["yf"], b + 1)
                if b + 1 < B:
                    modulate(b + 1)
                eng.wait_ge(S_["fo_ps"], b + 1)
                link(film(U[1], PS[:, 6, :], BFO[:, 0, :]))
                link(film(U[3], PS[:, 7, :], BFO[:, 1, :]))
                eng.wait_ge(S_["y_ps"], b + 1)
                link(tt(U[1], PS[:, 2, :], U[1], mul))
                link(tt(U[1], U[1], U[3], add))
                link(tt(XT[:, b, :], XT[:, b, :], U[1], add))
                eng.memset(EV3[:, :], 0.0).then_inc(S_["x3"], 1)
            layernorm(XT, XL, VEC["g_ffn"], VEC["b_ffn"], done="xl")
            for b in range(B):
                link(tt(XT[:, b, :], XT[:, b, :], VEC["b2"], add))
            for b in range(B):
                eng.wait_ge(S_["f2_ps"], b + 1)
                tt(XT[:, b, :], XT[:, b, :], PS[:, b, :], add).then_inc(S_["f2_sb"], 1)
            eng.wait_ge(S_["f2_sb"], B)
            layernorm(XT, XL, VEC["g_out"], VEC["b_out"])
            for b in range(B):
                link(tt(X[:, b, :], X[:, b, :], XL[:, b, :], add))
            layernorm(X, XL, done="xl")
            for u in range(NH + 1):
                if u < NH:
                    p = PB[u % 3]
                    eng.wait_ge(S_["as_ps"], u + 1)
                    if u >= 3:
                        eng.wait_ge(S_["pt_ps"], u - 2)
                    m = c("causal").unsqueeze(1).broadcast_to([P, B, T])
                    link(eng.scalar_tensor_tensor(out=p, in0=PS[:, 4 + u % 2, :].rearrange("p (a b) -> p a b", b=T),
                                                  scalar=SCALE, in1=m, op0=mul, op1=add))
                    link(eng.reduce_max(WS[:, :, 0], p, AX.X))
                    tt(p, p, WS[:, :, 0:1].broadcast_to([P, B, T]), sub).then_inc(S_["a_shift"], 1)
                if u:
                    v = u - 1
                    p = PB[v % 3]
                    eng.wait_ge(S_["a_exp"], v + 1)
                    link(eng.reduce_sum(WS[:, :, 1], p, AX.X))
                    link(eng.reciprocal(WS[:, :, 2], WS[:, :, 1]))
                    tt(p, p, WS[:, :, 2:3].broadcast_to([P, B, T]), mul).then_inc(S_["a_norm"], 1)
            for b in range(B):
                eng.wait_ge(S_["o_ps"], b + 1)
                link(tt(X[:, b, :], X[:, b, :], PS[:, 4 + b, :], add))
            layernorm(X, XL, done="xl")
            eng.wait_ge(S_["probs"], 1)
            for b in range(B):
                link(eng.max(V8[:, b, :], PR[:, b, :]))
                link(eng.max_index(I8[:, b, :], V8[:, b, :], PR[:, b, :]))
            link(eng.tensor_copy(I8F[:, :, :], I8[:, :, 0:2]))
            for k in range(2):
                link(tt(OH[:, :, k, :], c("expert").unsqueeze(1).broadcast_to([P, B, E]),
                        I8F[:, :, k:k + 1].broadcast_to([P, B, E]), ALU.is_equal))
            tt(PICK[:, :, :], OH[:, :, 0, :], OH[:, :, 1, :], add).then_inc(S_["pick"], 1)
            eng.wait_ge(S_["pick"], 1)
            eng.wait_ge(S_["rk_ps"], 1)
            link(eng.tensor_copy(RK[:, :, :], PS[:, 6, 0:B * E].rearrange("p (a b) -> p a b", b=E)))
            link(ts(RT[:, :, :], RK[:, :, :], 1.0, None, add))
            link(tt(RT[:, :, :], RT[:, :, :], PICK[:, :, :], mul))
            link(ts(RT[:, :, :], RT[:, :, :], -1.0, None, add))
            for b in range(B):
                tt(ONEH[:, b, :, :], c("slot").unsqueeze(1).broadcast_to([P, E, CAP]),
                   RT[:, b, :].unsqueeze(2).broadcast_to([P, E, CAP]), ALU.is_equal).then_inc(S_["oneh"], 1)
            eng.wait_ge(S_["oneh"], B)
            for k in range(2):
                link(tt(RT[:, :, :], RK[:, :, :], OH[:, :, k, :], mul))
                link(eng.reduce_sum(R2[:, :, k], RT[:, :, :], AX.X))
            link(ts(SL[:, :, :], R2[:, :, :], float(CAP - 1), None, ALU.min))
            link(eng.scalar_tensor_tensor(out=SL[:, :, :], in0=I8F[:, :, :], scalar=float(CAP), in1=SL[:, :, :],
                                          op0=mul, op1=add))
            eng.tensor_copy(SLU[:, :, :], SL[:, :, :]).then_inc(S_["slots"], 1)
            link(tt(WS[:, :, 0], V8[:, :, 0], V8[:, :, 1], add))
            link(ts(WS[:, :, 0], WS[:, :, 0], 1e-6, None, add))
            link(eng.reciprocal(WS[:, :, 0], WS[:, :, 0]))
            link(tt(WT2[:, :, :], V8[:, :, 0:2], WS[:, :, 0:1].broadcast_to([P, B, 2]), mul))
            link(ts(R2[:, :, :], R2[:, :, :], float(CAP), None, ALU.is_lt))
            link(tt(WT2[:, :, :], WT2[:, :, :], R2[:, :, :], mul))
            for e in range(E):
                for j in range(2):
                    eng.wait_ge(S_["ht_ps"], 2 * e + j + 1)
                    if e >= 2:
                        eng.wait_ge(S_["m2_ps"], e - 1)
                    eng.tensor_copy(HT[e % 2][:, 4 * j:4 * j + 4, :], PS[:, 6 + j, 0:4 * CAP]
                                    .rearrange("p (a b) -> p a b", b=CAP)).then_inc(S_["ht_sb"], 1)
            eng.wait_ge(S_["ld_g"], 16 * 8)
            for b in range(B):
                for k in range(2):
                    last = eng.scalar_tensor_tensor(out=X[:, b, :], in0=GA[:, b, k, :], scalar=WT2[:, b, k:k + 1],
                                                    in1=X[:, b, :], op0=mul, op1=add)
                    if k == 0:
                        link(last)
                last.then_inc(S_["fin"], 1)

        @block.tensor
        def _(eng):
            mm = eng.matmul

            def tr(dst, src, rows=P, **kw):
                return eng.transpose(dst, src, c("ident", rows)[:, 0:rows])

            def transposes(src, first=0):
                for b in range(4):
                    for k in range(4):
                        last = tr(PS[:, first + k, b * P:(b + 1) * P], src[:, b, k * P:(k + 1) * P])
                last.then_inc(S_["tr_ps"], 1)

            def context_keys(b):
                for k in range(GC):
                    n = b * GC + k
                    eng.wait_ge(S_[f"ld_cxt{k}"], 16 * (b + 1))
                    if n:
                        eng.wait_ge(S_["kt_sb"], n)
                    for j in range(KV):
                        last = mm(PS[:, 3, :], WK[:, j, :], CXT[:, j, k * 512:(k + 1) * 512],
                                  start=j == 0, stop=j == KV - 1)
                    last.then_inc(S_["kt_ps"], 1)

            def scores(i):
                b, h = divmod(i, XH)
                r = slice(DH * h, DH * h + DH)
                eng.wait_ge(S_["kt_sb"], GC * (b + 1))
                eng.wait_ge(S_["mask_row"], b + 1)
                for k in range(GC):
                    n = GC * i + k
                    if n >= 2:
                        eng.wait_ge(S_["s_sb"], n - 1)
                    cols = slice(k * 512, k * 512 + 512)
                    mm(PS[:, 4 + k % 2, :], QT[r, b * T:(b + 1) * T], KT[r, cols], start=True, stop=False)
                    mm(PS[:, 4 + k % 2, :], ONEB[DH * h:DH * h + 1, :], MROW[DH * h:DH * h + 1, cols],
                       start=False, stop=True).then_inc(S_["s_ps"], 1)

            def attended(b):
                eng.wait_ge(S_["d_done"], XH * (b + 1))
                eng.wait_ge(S_["diag"], 4 * (b + 1))
                for k in range(4):
                    if k >= 2:
                        eng.wait_ge(S_["at_sb"], 4 * b + k - 1)
                    for g in range(4):
                        n = 4 * k + g
                        last = tr(PS[:, 6 + k % 2, g * P:(g + 1) * P], DS[:, n * P:(n + 1) * P])
                    last.then_inc(S_["at_ps"], 1)
                eng.wait_ge(S_["at_sb"], 4 * (b + 1))
                if b + 1 < B:
                    eng.wait_ge(S_["kt_sb"], GC * (b + 2))
                for g in range(GT):
                    if g % 4 == 0:
                        eng.wait_ge(S_[f"ld_ctx{g // 4}"], 16 * (b + 1))
                    last = mm(PS[:, 3, 0:DV], AT[:, g, :], CTX[:, g, :], start=g == 0, stop=g == GT - 1)
                last.then_inc(S_["cc_ps"], 1)
                eng.wait_ge(S_["cc_sb"], b + 1)
                for k in range(KV):
                    last = tr(PS[:, 3, k * P:(k + 1) * P], CC[:, k * P:(k + 1) * P])
                last.then_inc(S_["cct_ps"], 1)

            def lags(q):
                eng.wait_ge(S_["powers"], q + 1)
                if q:
                    eng.wait_ge(S_["at_sb"], 4 * q)
                for j in range(4):
                    if j >= 2:
                        eng.wait_ge(S_["diag"], 4 * q + j - 1)
                    for g in range(2):
                        grp = 2 * j + g
                        d = slice(grp * 16, grp * 16 + 16)
                        last = mm(PS[:, 6 + j % 2, g * 256:(g + 1) * 256], PM[:, grp, :, :].rearrange("p a m -> p (a m)"), ZT[:, :, d],
                                  start=True, stop=True)
                    last.then_inc(S_["g_ps"], 1)

            eng.wait_ge(S_["ld_c"], 16)
            eng.wait_ge(S_["xt"], B)
            transposes(XT)
            eng.wait_ge(S_["tr_sb"], 4)
            eng.wait_ge(S_["ld_w"], 32)
            for k in range(KD):
                last = mm(PS[:, 4, :], WQ[:, k, :], TT[:, k, :], start=k == 0, stop=k == KD - 1)
            last.then_inc(S_["q_ps"], 1)
            context_keys(0)
            eng.wait_ge(S_["q_sb"], 1)
            scores(0)
            scores(1)
            for i in range(1, NT + 1):
                if i % 4 == 0:
                    lags(i // 4 - 1)
                    attended(i // 4 - 1)
                if i + 1 < NT:
                    scores(i + 1)
                if i % 4 == 2 and i // 4 + 1 < B:
                    if i // 4:
                        eng.wait_ge(S_["cct_sb"], i // 4)
                    context_keys(i // 4 + 1)
            eng.wait_ge(S_["kraw"], 1)
            for k in range(KD):
                last = tr(PS[:, 0, k * P:(k + 1) * P], KRAW[:, k, :])
            last.then_inc(S_["kt2_ps"], 1)
            eng.wait_ge(S_["ktd"], 1)
            eng.wait_ge(S_["cct_sb"], B)
            for n, m in enumerate(("fxa", "fkp", "fkb")):
                last = mm(PS[:, 1 + n, :], c(m), KTD[:, :], start=True, stop=True)
            last.then_inc(S_["spec_ps"], 1)
            eng.wait_ge(S_["ld_wv"], 16)
            for k in range(KD):
                for j in range(KV):
                    last = mm(PS[:, 4 + k, :], WV[:, j, k * P:(k + 1) * P], CCT[:, j, :], start=j == 0, stop=j == KV - 1)
            last.then_inc(S_["ct_ps"], 1)
            eng.wait_ge(S_["ct_sb"], KD)
            eng.wait_ge(S_["ld_wfi"], 16)

            def film(b, w, bank, sem):
                for j in range(2):
                    for k in range(KD):
                        last = mm(PS[:, bank + j, :], TT[:, k, b * T:(b + 1) * T], w[:, k, j * D:(j + 1) * D],
                                  start=k == 0, stop=k == KD - 1)
                last.then_inc(S_[sem], 1)

            film(0, WFI, 4, "fi_ps")
            eng.wait_ge(S_["spec"], 3)
            for b in range(B):
                eng.wait_ge(S_["x2"], b + 1)
                for n, m in enumerate(("fxa", "fxb")):
                    last = mm(PS[:, n, :], c(m), XL[:, b, :], start=True, stop=True)
                last.then_inc(S_["xf_ps"], 1)
                if b + 1 < B:
                    film(b + 1, WFI, 4, "fi_ps")
                if b:
                    eng.wait_ge(S_["x3"], b)
                if b == 0:
                    eng.wait_ge(S_["ld_wfo"], 16)
                film(b, WFO, 6, "fo_ps")
                eng.wait_ge(S_["yf"], b + 1)
                mm(PS[:, 2, :], c("ga"), U[0], start=True, stop=False)
                mm(PS[:, 2, :], c("gb"), U[2], start=False, stop=True).then_inc(S_["y_ps"], 1)
            eng.wait_ge(S_["x3"], B)
            eng.wait_ge(S_["xl"], B)
            transposes(XL)
            eng.wait_ge(S_["tr_sb"], 8)
            eng.wait_ge(S_["ld_w1"], 16)
            for f in range(HID // P):
                if f >= 4:
                    eng.wait_ge(S_["gelu"], f - 3)
                for k in range(KD):
                    last = mm(PS[:, 4 + f % 4, :], W1[:, k, f * P:(f + 1) * P], TT[:, k, :], start=k == 0, stop=k == KD - 1)
                last.then_inc(S_["f1_ps"], 1)
            eng.wait_ge(S_["ld_w2"], 16)
            eng.wait_ge(S_["gelu"], HID // P)
            for b in range(B):
                for f in range(HID // P):
                    last = mm(PS[:, b, :], GEL[:, f, b * T:(b + 1) * T], W2[:, f, :], start=f == 0, stop=f == HID // P - 1)
                last.then_inc(S_["f2_ps"], 1)
            eng.wait_ge(S_["f2_sb"], B)
            eng.wait_ge(S_["xl"], 2 * B)
            transposes(XL)
            eng.wait_ge(S_["tr_sb"], 12)
            for n in range(4):
                eng.wait_ge(S_[f"ld_attn{n}"], 16)
            for n in range(12):
                a, m = divmod(n, 4)
                if n >= 4:
                    eng.wait_ge(S_["qkv_sb"], n - 3)
                for k in range(KD):
                    blk = slice(m * P, (m + 1) * P)
                    if a < 2:
                        last = mm(PS[:, 4 + m, :], WTR[:, a, k, blk], TT[:, k, :], start=k == 0, stop=k == KD - 1)
                    else:
                        last = mm(PS[:, 4 + m, :], TT[:, k, blk], WTR[:, a, k, :], start=k == 0, stop=k == KD - 1)
                last.then_inc(S_["qkv_ps"], 1)
            eng.wait_ge(S_["qkv_sb"], 12)

            def head_scores(u):
                blk, r = u // 4, slice(DH * (u % 4), DH * (u % 4) + DH)
                if u >= 2:
                    eng.wait_ge(S_["a_shift"], u - 1)
                for b in range(B):
                    t = slice(b * T, (b + 1) * T)
                    last = mm(PS[:, 4 + u % 2, t], QA[r, blk, t], KS[r, blk, t], start=True, stop=True)
                last.then_inc(S_["as_ps"], 1)

            def head_values(u):
                eng.wait_ge(S_["pt_sb"], u + 1)
                for b in range(B):
                    last = mm(PS[DH * (u % 4):DH * (u % 4) + DH, u // 4, b * T:(b + 1) * T],
                              VA[:, b, DH * u:DH * u + DH], PBT[u % 2][:, b, :], start=True, stop=True)
                last.then_inc(S_["av_ps"], 1)

            head_scores(0)
            head_scores(1)
            for u in range(NH):
                if u + 2 < NH:
                    head_scores(u + 2)
                eng.wait_ge(S_["a_norm"], u + 1)
                if u >= 2:
                    eng.wait_ge(S_["pt_sb"], u - 1)
                for b in range(B):
                    last = tr(PS[:, 6 + u % 2, b * P:(b + 1) * P], PB[u % 3][:, b, :])
                last.then_inc(S_["pt_ps"], 1)
                head_values(u)
            eng.wait_ge(S_["ao_sb"], 4)
            for b in range(B):
                for k in range(KD):
                    last = mm(PS[:, 4 + b, :], TT[:, k, b * T:(b + 1) * T], WTR[:, 3, k, :], start=k == 0, stop=k == KD - 1)
                last.then_inc(S_["o_ps"], 1)
            eng.wait_ge(S_["xl"], 3 * B)
            transposes(XL)
            eng.wait_ge(S_["ld_small"], 16 * 5)
            eng.wait_ge(S_["tr_sb"], 16)
            for b in range(B):
                for k in range(KD):
                    last = mm(PS[:, 5, b * E:(b + 1) * E], TT[:, k, b * T:(b + 1) * T], GWT[:, k, :],
                              start=k == 0, stop=k == KD - 1)
            last.then_inc(S_["lg_ps"], 1)
            eng.wait_ge(S_["pick"], 1)
            for b in range(B):
                for j in range(b + 1):
                    last = mm(PS[:, 6, b * E:(b + 1) * E], c("tri" if j == b else "ones"), PICK[:, j, :],
                              start=j == 0, stop=j == b)
            last.then_inc(S_["rk_ps"], 1)
            eng.wait_ge(S_["oneh"], B)
            for ch in range(3):
                for k in range(KD):
                    n = 4 * ch + k
                    if n >= 4:
                        eng.wait_ge(S_["xe_sb"], n - 3)
                    e0, e1 = CHUNK[ch], CHUNK[ch + 1]
                    for b in range(B):
                        last = mm(PS[:, k, 0:(e1 - e0) * CAP], XL[:, b, k * P:(k + 1) * P],
                                  ONEH[:, b, e0:e1, :], start=b == 0, stop=b == B - 1)
                    last.then_inc(S_["xe_ps"], 1)
            eng.wait_ge(S_["xe_sb"], 12)

            def expert_up(e):
                eng.wait_ge(S_[f"ld_e1{e % 2}"], 16 * (e // 2 + 1))
                if e:
                    eng.wait_ge(S_["h_sb"], 2 * e)
                for j in range(2):
                    for k in range(KD):
                        last = mm(PS[0:CAP, 4 + j, :], XET[:, k, e * CAP:(e + 1) * CAP],
                                  EW1[e % 2][:, k, 512 * j:512 * j + 512], start=k == 0, stop=k == KD - 1)
                last.then_inc(S_["m1_ps"], 1)

            expert_up(0)
            for e in range(E):
                eng.wait_ge(S_["h_sb"], 2 * (e + 1))
                for j in range(2):
                    if e:
                        eng.wait_ge(S_["ht_sb"], 2 * (e - 1) + j + 1)
                    for f in range(4):
                        k = 4 * j + f
                        last = tr(PS[:, 6 + j, f * CAP:(f + 1) * CAP], H[e % 2][0:CAP, k * P:(k + 1) * P], rows=CAP)
                    last.then_inc(S_["ht_ps"], 1)
                if e + 1 < E:
                    expert_up(e + 1)
                eng.wait_ge(S_["ht_sb"], 2 * (e + 1))
                eng.wait_ge(S_[f"ld_e2{e % 2}"], 16 * (e // 2 + 1))
                if e >= 2:
                    eng.wait_ge(S_["y_sb"], e - 1)
                for f in range(F // P):
                    last = mm(PS[0:CAP, e % 2, :], HT[e % 2][:, f, :], EW2[e % 2][:, f, :],
                              start=f == 0, stop=f == F // P - 1)
                last.then_inc(S_["m2_ps"], 1)


_ARGS = {"x": "x", "ctx": "ctx_768", "ctxT": "ctx_768", "mask_x": "mask_BxS_bf1", "mask_ctx": "mask_BxS2_bf1",
         "Wq": "L0_xattn_Wq", "Wk": "L0_xattn_Wk", "Wv": "L0_xattn_Wv", "W_film_in": "L0_xattn_W_film_in",
         "b_film_in": "L0_xattn_b_film_in", "W_film_out": "L0_xattn_W_film_out",
         "b_film_out": "L0_xattn_b_film_out", "g_in": "L0_xattn_g_norm_in", "b_in": "L0_xattn_b_norm_in",
         "g_out": "L0_xattn_g_norm_out", "b_out": "L0_xattn_b_norm_out", "g_ffn": "L0_xattn_g_ffn",
         "b_ffn": "L0_xattn_b_ffn", "W1": "L0_xattn_W1", "b1": "L0_xattn_b1", "W2": "L0_xattn_W2",
         "b2": "L0_xattn_b2", "log_dt": "L0_xattn_log_dt", "A_re": "L0_xattn_A_re", "A_im": "L0_xattn_A_im",
         "C_re": "L0_xattn_C_re", "C_im": "L0_xattn_C_im", "D_skip": "L0_xattn_D_skip",
         "mod_gate": "L0_xattn_mod_gate", "Aq": "L0_attn_Wq", "Ak": "L0_attn_Wk", "Av": "L0_attn_Wv",
         "Ao": "L0_attn_Wo", "gate_w": "L0_ffn_gate_w", "w1": "L0_ffn_w1", "w2": "L0_ffn_w2"}


def kernel(**inputs):
    import numpy as _np
    import concourse.bacc as _bacc
    from concourse import mybir as _mybir
    from concourse.bass_utils import run_bass_kernel_spmd as _run

    nc = _bacc.Bacc("TRN2", target_bir_lowering=False, num_devices=1)
    arrays, aps = {}, {}
    for name, arg in _ARGS.items():
        a = _np.asarray(inputs[arg])
        if name in ("A_re", "A_im", "C_re", "C_im", "Aq", "Ak", "Av", "Ao", "gate_w", "mask_x"):
            a = a.T
        if name in ("D_skip", "b1"):
            a = a.reshape(-1, P).T
        if name == "ctxT":
            a = a.transpose(0, 2, 1)
        a = _np.ascontiguousarray(a)
        if a.dtype == _np.bool_:
            a = a.view(_np.uint8)
        if a.ndim == 0:
            a = a.reshape(1)
        arrays[f"in_{name}"] = a
        aps[name] = nc.dram_tensor(f"in_{name}", a.shape, _mybir.dt.from_np(a.dtype), kind="ExternalInput").ap()
    arrays["in_consts"] = shape_constants()
    aps["consts"] = nc.dram_tensor("in_consts", (P, NCONST), _mybir.dt.float32, kind="ExternalInput").ap()
    out = nc.dram_tensor("out", (B, T, D), _mybir.dt.float32, kind="ExternalOutput").ap()
    yrows = nc.dram_tensor("expert_rows", (NSLOT, D), _mybir.dt.float32, kind="Internal").ap()
    kdram = nc.dram_tensor("s4d_kernel", (D, LA * LB), _mybir.dt.float32, kind="Internal").ap()
    build(nc, aps, out, yrows, kdram)
    r = _run(nc, [arrays], core_ids=[0])
    return r.results[0]["out"]
```
